# Optimizing a Trainium2 kernel written in Bass

```python
import numpy as np
import jax
import jax.numpy as jnp

def _softmax(x, axis=-1):
    return jax.nn.softmax(x, axis=axis)

def _gelu(x):
    return jax.nn.gelu(x, approximate=True)

def _silu(x):
    return jax.nn.silu(x)

def _sigmoid(x):
    return jax.nn.sigmoid(x)

def _layernorm(x, axis=-1, eps=1e-05):
    m = jnp.mean(x, axis=axis, keepdims=True)
    v = jnp.var(x, axis=axis, keepdims=True)
    return (x - m) / jnp.sqrt(v + eps)

def _scatter_add(tgt, idx, src, axis=0):
    return tgt.at[idx].add(src)

def _segment_sum(src, seg, n):
    return jax.ops.segment_sum(src, seg, n)
kernel_name = 'mk_adj_resnorm_d2_adj_r2_01cb90'

def setup_inputs(seed: int=0):
    np.random.seed(seed)
    _w = jnp.asarray

    def _rec_inputs():
        import jax
        import jax.numpy as jnp
        _gk = jax.random.key(seed)
        x = -0.0003929 + 0.9999 * jax.random.normal(jax.random.fold_in(_gk, 1), (128, 128, 128), jnp.float32)
        _a = jax.random.bernoulli(jax.random.fold_in(_gk, 2), 0.125, (128, 128))
        _a = jnp.logical_or(_a, jnp.swapaxes(_a, -1, -2))
        _a = jnp.logical_or(_a, jnp.eye(128, dtype=bool))
        _af = _a.astype(jnp.float32)
        _af = _af * jax.random.uniform(jax.random.fold_in(_gk, 3), (128, 128), jnp.float32, 0.05, 1)
        adj = _af
        return (x, adj)
    x, adj = _rec_inputs()

    def _L0_gnn_setup():
        import jax, jax.numpy as jnp
        import numpy as np
        EPS = 1e-05

        def _batchnorm(x, gamma, beta):
            mu = jnp.mean(x, axis=0)
            var = jnp.var(x, axis=0)
            return (x - mu) * jax.lax.rsqrt(var + EPS) * gamma + beta
        key = jax.random.key(seed)
        ks = jax.random.split(key, 4)
        b, n, d, h, o = (32, 1024, 128, 256, 128)
        features = jax.random.normal(ks[0], (b, n, d), dtype=jnp.float32)
        A = jax.random.uniform(ks[1], (n, n), dtype=jnp.float32)
        lim1 = float(np.sqrt(6.0 / (d + h)))
        W1 = jax.random.uniform(ks[2], (h, d), minval=-lim1, maxval=lim1, dtype=jnp.float32)
        b1 = jnp.zeros((h,), jnp.float32)
        lim2 = float(np.sqrt(6.0 / (h + o)))
        W2 = jax.random.uniform(ks[3], (o, h), minval=-lim2, maxval=lim2, dtype=jnp.float32)
        b2 = jnp.zeros((o,), jnp.float32)
        g1 = jnp.ones((h,), jnp.float32)
        be1 = jnp.zeros((h,), jnp.float32)
        g2 = jnp.ones((o,), jnp.float32)
        be2 = jnp.zeros((o,), jnp.float32)
        return {'features': features, 'A': A, 'W1': W1, 'b1': b1, 'g1': g1, 'be1': be1, 'W2': W2, 'b2': b2, 'g2': g2, 'be2': be2}
    _L0_gnn_all = _L0_gnn_setup()
    _L0_gnn_in = {k: v for k, v in _L0_gnn_all.items() if k in ('W1', 'b1', 'g1', 'be1', 'W2', 'b2', 'g2', 'be2')}
    del _L0_gnn_all

    def _L1_gnn_setup():
        import jax, jax.numpy as jnp
        import numpy as np
        B, T, D, H = (64, 1024, 128, 128)
        MAX_SKIP = 4

        def _lstm_last(Wih, Whh, bih, bhh, xs):
            N, _, Hd = xs.shape
            bias = bih + bhh

            def step(carry, x_t):
                h, c = carry
                g = x_t @ Wih.T + h @ Whh.T + bias
                i, f, gg, o = jnp.split(g, 4, axis=-1)
                c = jax.nn.sigmoid(f) * c + jax.nn.sigmoid(i) * jnp.tanh(gg)
                h = jax.nn.sigmoid(o) * jnp.tanh(c)
                return ((h, c), None)
            init = (jnp.zeros((N, Hd), xs.dtype), jnp.zeros((N, Hd), xs.dtype))
            (h_last, _), _ = jax.lax.scan(step, init, jnp.swapaxes(xs, 0, 1))
            return h_last
        key = jax.random.key(seed)
        ks = jax.random.split(key, 8)
        s = 0.05
        x = jax.random.normal(ks[0], (B, T, D), jnp.float32)
        adj = jax.random.uniform(ks[1], (T, T), jnp.float32) / T
        Wg0 = jax.random.normal(ks[2], (D, H), jnp.float32) * s
        bg0 = jnp.zeros((H,), jnp.float32)
        Wg1 = jax.random.normal(ks[3], (H, H), jnp.float32) * s
        bg1 = jnp.zeros((H,), jnp.float32)
        Wih = jax.random.normal(ks[4], (MAX_SKIP, 4 * H, H), jnp.float32) * s
        Whh = jax.random.normal(ks[5], (MAX_SKIP, 4 * H, H), jnp.float32) * s
        bih = jax.random.normal(ks[6], (MAX_SKIP, 4 * H), jnp.float32) * s
        bhh = jax.random.normal(ks[7], (MAX_SKIP, 4 * H), jnp.float32) * s
        return dict(x=x, adj=adj, Wg0=Wg0, bg0=bg0, Wg1=Wg1, bg1=bg1, Wih=Wih, Whh=Whh, bih=bih, bhh=bhh)
    _L1_gnn_all = _L1_gnn_setup()
    _L1_gnn_in = {k: v for k, v in _L1_gnn_all.items() if k in ('Wg0', 'bg0', 'Wg1', 'bg1', 'Wih', 'Whh', 'bih', 'bhh')}
    del _L1_gnn_all
    return {'x': x, 'adj': adj, 'L0_gnn_W1': _L0_gnn_in['W1'], 'L0_gnn_b1': _L0_gnn_in['b1'], 'L0_gnn_g1': _L0_gnn_in['g1'], 'L0_gnn_be1': _L0_gnn_in['be1'], 'L0_gnn_W2': _L0_gnn_in['W2'], 'L0_gnn_b2': _L0_gnn_in['b2'], 'L0_gnn_g2': _L0_gnn_in['g2'], 'L0_gnn_be2': _L0_gnn_in['be2'], 'L1_gnn_Wg0': _L1_gnn_in['Wg0'], 'L1_gnn_bg0': _L1_gnn_in['bg0'], 'L1_gnn_Wg1': _L1_gnn_in['Wg1'], 'L1_gnn_bg1': _L1_gnn_in['bg1'], 'L1_gnn_Wih': _L1_gnn_in['Wih'], 'L1_gnn_Whh': _L1_gnn_in['Whh'], 'L1_gnn_bih': _L1_gnn_in['bih'], 'L1_gnn_bhh': _L1_gnn_in['bhh']}

def reference(x, adj, L0_gnn_W1, L0_gnn_b1, L0_gnn_g1, L0_gnn_be1, L0_gnn_W2, L0_gnn_b2, L0_gnn_g2, L0_gnn_be2, L1_gnn_Wg0, L1_gnn_bg0, L1_gnn_Wg1, L1_gnn_bg1, L1_gnn_Wih, L1_gnn_Whh, L1_gnn_bih, L1_gnn_bhh):
    import jax
    import jax.numpy as jnp

    def _L0_gnn_ref(features, A, W1, b1, g1, be1, W2, b2, g2, be2):
        import jax, jax.numpy as jnp
        import numpy as np
        EPS = 1e-05

        def _batchnorm(x, gamma, beta):
            mu = jnp.mean(x, axis=0)
            var = jnp.var(x, axis=0)
            return (x - mu) * jax.lax.rsqrt(var + EPS) * gamma + beta
        b, n, d = features.shape
        A_norm = A + jnp.eye(n, dtype=A.dtype)
        deg = jnp.sum(A_norm, axis=0) + jnp.sum(A_norm, axis=1) - jnp.diagonal(A_norm)
        dinv = jax.lax.rsqrt(deg)
        A_hat = A_norm * dinv[:, None] * dinv[None, :]
        agg = jnp.einsum('nm,bmd->bnd', A_hat, features)
        x = agg.reshape(-1, d)
        h = jax.nn.relu(_batchnorm(x @ W1.T + b1, g1, be1))
        out = h @ W2.T + b2
        out = _batchnorm(out, g2, be2)
        return out.reshape(b, n, -1)

    def _L1_gnn_ref(x, adj, Wg0, bg0, Wg1, bg1, Wih, Whh, bih, bhh):
        import jax, jax.numpy as jnp
        import numpy as np
        B, T, D, H = (64, 1024, 128, 128)
        MAX_SKIP = 4

        def _lstm_last(Wih, Whh, bih, bhh, xs):
            N, _, Hd = xs.shape
            bias = bih + bhh

            def step(carry, x_t):
                h, c = carry
                g = x_t @ Wih.T + h @ Whh.T + bias
                i, f, gg, o = jnp.split(g, 4, axis=-1)
                c = jax.nn.sigmoid(f) * c + jax.nn.sigmoid(i) * jnp.tanh(gg)
                h = jax.nn.sigmoid(o) * jnp.tanh(c)
                return ((h, c), None)
            init = (jnp.zeros((N, Hd), xs.dtype), jnp.zeros((N, Hd), xs.dtype))
            (h_last, _), _ = jax.lax.scan(step, init, jnp.swapaxes(xs, 0, 1))
            return h_last
        h = jax.nn.relu(jnp.einsum('ts,bsh->bth', adj, x @ Wg0 + bg0))
        h = jax.nn.relu(jnp.einsum('ts,bsh->bth', adj, h @ Wg1 + bg1))
        Bv, Tv, Hd = h.shape
        for p in range(1, MAX_SKIP + 1):
            nw = Tv // p
            wins = h[:, :nw * p, :].reshape(Bv * nw, p, Hd)
            last = _lstm_last(Wih[p - 1], Whh[p - 1], bih[p - 1], bhh[p - 1], wins)
            idx = jnp.arange(nw) * p + (p - 1)
            h = h.at[:, idx, :].set(last.reshape(Bv, nw, Hd))
        return h
    x = _layernorm(x + _L0_gnn_ref(x, adj, L0_gnn_W1, L0_gnn_b1, L0_gnn_g1, L0_gnn_be1, L0_gnn_W2, L0_gnn_b2, L0_gnn_g2, L0_gnn_be2), axis=-1)
    x = _layernorm(x + _L1_gnn_ref(x, adj, L1_gnn_Wg0, L1_gnn_bg0, L1_gnn_Wg1, L1_gnn_bg1, L1_gnn_Wih, L1_gnn_Whh, L1_gnn_bih, L1_gnn_bhh), axis=-1)
    return x

_drawn_inputs = setup_inputs


def setup_inputs(seed=0):
    import zlib

    import numpy as np

    out = dict(_drawn_inputs(seed))
    spreads = {'L0_gnn_b1': (0.0, 0.8),
     'L0_gnn_g1': (1.0, 0.2),
     'L0_gnn_be1': (0.0, 0.1),
     'L0_gnn_b2': (0.0, 0.8),
     'L0_gnn_g2': (1.0, 0.2),
     'L0_gnn_be2': (0.0, 0.1),
     'L1_gnn_bg0': (0.0, 0.1),
     'L1_gnn_bg1': (0.0, 0.1)}
    factors = {'L1_gnn_Whh': 7.666, 'L1_gnn_bih': 3.078, 'L1_gnn_bhh': 3.129}
    for name, (base, spread) in spreads.items():
        noise = np.random.default_rng([zlib.crc32(name.encode()), seed]).standard_normal(out[name].shape)
        drawn = base * np.exp(spread * noise) if base else spread * noise
        out[name] = jnp.asarray(drawn.astype(out[name].dtype))
    for name, factor in factors.items():
        out[name] = (out[name] * factor).astype(out[name].dtype)
    return out
```

```python
from contextlib import ExitStack

import numpy as np

import concourse.bass as bass
from concourse import mybir

ALU = mybir.AluOpType
ACT = mybir.ActivationFunctionType
AX_X = mybir.AxisListType.X
F32 = mybir.dt.float32
F16 = mybir.dt.float16

P = 128
BANK = 512
CB = BANK // P
GB = 2 * CB
EPS = 1e-5
W_SCALE = 16.0
I, F, G, O = range(4)

EARLY_STEPS = [
    dict(p=1, first=True, b0=0, nb=CB, row=0, rows=P, last=True),
    dict(p=1, first=True, b0=CB, nb=CB, row=0, rows=P, last=True),
    dict(p=2, first=True, b0=0, nb=GB, row=0, rows=P // 2, last=False),
    dict(p=2, first=False, b0=0, nb=GB, row=1, rows=P // 2, last=True),
]
LATE_STEPS = [dict(p=p, first=s == 0, b0=0, nb=GB, row=s, rows=P // p, last=s == p - 1)
              for p in (3, 4) for s in range(p)]


def gates_of(step):
    return (G, I, O) if step["first"] else (G, I, F, O)


def rows_of(tensor, step):
    p, row = step["p"], step["row"]
    return tensor[:, step["b0"]:step["b0"] + step["nb"], row:row + p * (step["rows"] - 1) + 1:p]


def flat(buffer, step):
    return buffer[:, 0:step["nb"] * step["rows"]].rearrange("k (b t) -> k b t", b=step["nb"])


def resnorm_gnn_kernel(nc, x, adj, W1, b1, g1, be1, W2, b2, g2, be2,
                       Wg0, bg0, Wg1, bg1, Wih, Whh, bih, bhh, out):
    B = x.shape[0]
    H1 = W1.shape[0] // P
    CHUNKS = B // CB
    GROUPS = B // GB
    GCOLS = GB * P
    PERIODS = Wih.shape[0]
    NG = 4 * PERIODS
    assert x.shape[1:] == (P, P) and H1 == 2 and GROUPS % 2 == 0 and CHUNKS % 4 == 0

    x_rows = x.rearrange("b n d -> n b d")
    out_rows = out.rearrange("b n d -> n b d")
    x1_dram = nc.dram_tensor("x1_scratch", [P, B, P], F32, kind="Internal").ap()

    with ExitStack() as ctx:
        def sb(name, shape, dt=F32):
            return ctx.enter_context(nc.sbuf_tensor(name, shape, dt))

        def sem(name):
            return ctx.enter_context(nc.semaphore(name))

        ident = sb("ident", [P, P])
        ident16 = sb("ident16", [P, P], F16)
        ones = sb("ones", [P, P])
        minus_half = sb("minus_half", [P, GB])
        adj_n = sb("adj_n", [P, P])
        a_norm = sb("a_norm", [P, P])
        tmp_pp = sb("tmp_pp", [P, P])
        adjT = sb("adjT", [P, P])
        ahatT = sb("ahatT", [P, P])
        w1T = sb("w1T", [P, H1, P])
        w2T = sb("w2T", [P, H1, P])
        wg0_sb = sb("wg0_sb", [P, P])
        wg1_sb = sb("wg1_sb", [P, P])
        vec = sb("vec", [P, P])
        gate_bias = sb("gate_bias", [P, NG])
        small = sb("small", [P, 16])
        split16 = sb("split16", [P, 2, P], F16)
        bias_l = sb("bias_l", [P, 2, P], F16)
        bias_r = sb("bias_r", [P, CB, P], F16)
        wih = sb("wih", [P, 2, NG * P], F16)
        whh = sb("whh", [P, 2, (NG - 4) * P], F16)
        st1 = sb("st1", [P, H1, CHUNKS, 6])
        st2 = sb("st2", [P, CHUNKS, 6])
        mean_var = sb("mean_var", [P, 3, 2])
        bn_scale = sb("bn_scale", [P, 3])
        bn_shift = sb("bn_shift", [P, 3])
        bn_rstd = sb("bn_rstd", [P, 3])
        store = sb("store", [P, H1, B * P])
        area = store[:, 1, :].rearrange("p (k n) -> p k n", n=GCOLS)

        def group_buffer(k):
            return area[:, k, :].rearrange("p (b n) -> p b n", b=GB)

        def split_buffer(k):
            return area[:, k, :].bitcast(F16).rearrange("p (s b n) -> p s b n", s=2, b=GB)

        x_res = [group_buffer(0), group_buffer(1)]
        x1 = [group_buffer(2), group_buffer(3)]
        zT, y, u0T, h0T, u1, x1_back, y2, out_sb = (group_buffer(k) for k in range(4, 12))
        gnn16 = split_buffer(12)
        h16 = [split_buffer(13), split_buffer(14)]
        ln_stats = sb("ln_stats", [P, 2, GB, 6])
        ln_mv = sb("ln_mv", [P, 2, 3, GB])
        ln_coef = sb("ln_coef", [P, 2, 3, GB])

        ps = ctx.enter_context(nc.psum_tensor("ps", [P, 8, BANK], F32))

        ld_adj, ld_w12, ld_wg, ld_vec, ld_bg, ld_lstm = (
            sem(f"ld_{n}") for n in ("adj", "w12", "wg", "vec", "bg", "lstm"))
        consts_done, prep_pe, prep_dve, dinv_done = (
            sem(n) for n in ("consts_done", "prep_pe", "prep_dve", "dinv_done"))
        w_turned, w_hi_done, w_lo_done = sem("w_turned"), sem("w_hi_done"), sem("w_lo_done")
        x_loaded = [sem(f"x_loaded{k}") for k in range(4)]
        agg_summed, agg_copied = sem("agg_summed"), sem("agg_copied")
        chan_summed, chan_stored, chan_stats = sem("chan_summed"), sem("chan_stored"), sem("chan_stats")
        bn_moments, bn_rstd_done, bn_step, bn_ready = (
            sem("bn_moments"), sem("bn_rstd_done"), sem("bn_step"), sem("bn_ready"))
        relu_done, out_summed, out_stored, out_stats = (
            sem("relu_done"), sem("out_summed"), sem("out_stored"), sem("out_stats"))
        res_loaded = [sem("res_loaded0"), sem("res_loaded1")]
        z_ready, z_turned = sem("z_ready"), sem("z_turned")
        y_ready, y_stats, y_moments, x1_ready = (
            sem("y_ready"), sem("y_stats"), sem("y_moments"), sem("x1_ready"))
        x1_spilled = [sem("x1_spilled0"), sem("x1_spilled1")]
        u0_summed, u0_copied = sem("u0_summed"), sem("u0_copied")
        h0_summed, h0_copied = sem("h0_summed"), sem("h0_copied")
        u1_summed, u1_copied = sem("u1_summed"), sem("u1_copied")
        gnn_summed, gnn_hi_done, gnn_lo_done = sem("gnn_summed"), sem("gnn_hi_done"), sem("gnn_lo_done")
        x1_reloaded = sem("x1_reloaded")
        h_turned, y2_ready, y2_stats, y2_moments, out_ready, out_written = (
            sem("h_turned"), sem("y2_ready"), sem("y2_stats"), sem("y2_moments"),
            sem("out_ready"), sem("out_written"))
        ln_step, coef_seen = sem("ln_step"), sem("coef_seen")

        class Lstm:

            def __init__(self, name, steps, bank):
                self.steps, self.bank = steps, bank
                self.buf = sb(f"{name}_buf", [P, 10, BANK])
                self.acts = self.buf[:, 0:4, :]
                self.cell, self.ig, self.fc, self.tanh_c, self.hid = (self.buf[:, k, :] for k in range(4, 9))
                self.hid16 = self.buf[:, 9, :].bitcast(F16).rearrange("p (s n) -> p s n", s=2)
                self.gate_summed, self.gate_done, self.parts, self.cell_done, self.tanh_done, \
                    self.hid_done, self.hi_done, self.lo_done = (sem(f"{name}_{n}") for n in (
                        "gate_summed", "gate_done", "parts", "cell_done", "tanh_done", "hid_done",
                        "hi_done", "lo_done"))
                self.n_gates = sum(len(gates_of(s)) for s in steps)
                self.n_steps = len(steps)
                self.n_parts = 2 * sum(not s["first"] for s in steps)

            def gates_before(self, g, s):
                return g * self.n_gates + sum(len(gates_of(t)) for t in self.steps[:s])

            def steps_before(self, g, s):
                return g * self.n_steps + s

            def parts_before(self, g, s):
                return g * self.n_parts + 2 * sum(not t["first"] for t in self.steps[:s])

        early = Lstm("early", EARLY_STEPS, 0)
        late = Lstm("late", LATE_STEPS, 3)
        GATE_BANKS = 3
        TURN = 6

        relu1 = early.buf[:, 0:4, :].rearrange("p (q h) n -> p q h n", h=H1)
        aggT = early.buf[:, 4:6, :]
        x_in = early.buf[:, 6:10, :]
        blocks = late.buf[:, :, :].rearrange("p k (j n) -> p (k j) n", n=P)
        lstm_rows = blocks[:, 0:2 * NG - 4, :]
        w12_rows = blocks[:, 28:32, :]
        vec_rows = blocks[:, 32, :]
        bg_rows = blocks[:, 33:35, :]
        assert 2 * NG - 4 <= 28
        VB1, VG1, VBE1, VB2, VG2, VBE2, VIH, VHH = 0, 2, 4, 6, 7, 8, 9, 9 + NG
        N_CONSTS = 8
        MOMENT_STEPS = 5
        W_JOBS = (2 * NG - 4) // 4

        def split_weights(job):
            if job < PERIODS:
                return wih[:, :, job * BANK:(job + 1) * BANK]
            return whh[:, :, (job - PERIODS) * BANK:(job - PERIODS + 1) * BANK]

        def wait(eng, semaphore, count):
            if not isinstance(count, int) or count > 0:
                eng.wait_ge(semaphore, count)

        def third_phase(eng, body, peel_end=0):
            for it in range(4):
                body(it // 2, it % 2)
            with eng.Fori(2, GROUPS // 2 - peel_end) as k:
                for q in range(2):
                    body(k, q)
            for it in range(GROUPS - 2 * peel_end, GROUPS + 3):
                body(it // 2, it % 2)

        def runs(k, q, lag):
            return not isinstance(k, int) or 0 <= 2 * k + q - lag < GROUPS

        def chunks_by_four(eng, body):
            for c in range(4):
                body(c, c)
            with eng.Fori(1, CHUNKS // 4) as k:
                for q in range(4):
                    body(k * 4 + q, q)

        block = ctx.enter_context(nc.Block())

        @block.sync
        def _(sp):
            sp.dma_start(adj_n[:], adj).then_inc(ld_adj, 16)

            def load_x(c, slot):
                wait(sp, agg_summed, c - 3)
                sp.dma_start(x_in[:, slot, :].rearrange("p (b d) -> p b d", b=CB),
                             x_rows[:, bass.ds(c * CB, CB), :]).then_inc(x_loaded[slot], 16)

            sp.dma_start(w12_rows[:, 0:2, :], W1.rearrange("(j p) d -> p j d", p=P)).then_inc(ld_w12, 16)
            sp.dma_start(w12_rows[:, 2:4, :].rearrange("p j d -> p (j d)"), W2).then_inc(ld_w12, 16)
            for c in range(4):
                load_x(c, c)
            sp.wait_ge(consts_done, 1)
            for row, v in ((VB1, b1), (VG1, g1), (VBE1, be1), (VB2, b2), (VG2, g2), (VBE2, be2)):
                sp.dma_start(vec_rows[row:row + v.shape[0] // P, :],
                             v.rearrange("(r p) -> r p", p=P)).then_inc(ld_vec, 16)
            for row, v in ((VIH, bih), (VHH, bhh)):
                sp.dma_start(vec_rows[row:row + NG, :],
                             v.rearrange("a (r p) -> (a r) p", p=P)).then_inc(ld_vec, 16)
            for k, v in enumerate((bg0, bg1)):
                sp.dma_start(bg_rows[:, k, :], v.rearrange("(a n) -> a n", a=1).broadcast_to([P, P]))\
                    .then_inc(ld_bg, 16)
            sp.dma_start(wg0_sb[:], Wg0).then_inc(ld_wg, 16)
            sp.dma_start(wg1_sb[:], Wg1).then_inc(ld_wg, 16)
            sp.dma_start(lstm_rows[:, 0:NG, :], Wih.rearrange("a (g p) d -> p (a g) d", p=P)).then_inc(ld_lstm, 16)
            sp.dma_start(lstm_rows[:, NG:2 * NG - 4, :],
                         Whh[1:PERIODS].rearrange("a (g p) d -> p (a g) d", p=P)).then_inc(ld_lstm, 16)
            with sp.Fori(1, CHUNKS // 4) as k:
                for slot in range(4):
                    load_x(k * 4 + slot, slot)

            sp.wait_ge(relu_done, H1 * CHUNKS)

            def load_residual(g, par):
                wait(sp, y_ready, 2 * (g - 1))
                sp.dma_start(x_res[par], x_rows[:, bass.ds(g * GB, GB), :]).then_inc(res_loaded[par], 16)

            load_residual(0, 0)

            def body(k, q):
                it = 2 * k + q
                if runs(k, q, 3):
                    g, par = it - 3, 1 - q
                    sp.wait_ge(x1_spilled[par], 16 * (k + (q - 3) // 2 + 1))
                    sp.dma_start(x1_back, x1_dram[:, bass.ds(g * GB, GB), :]).then_inc(x1_reloaded, 16)
                if runs(k, q, -1):
                    load_residual(it + 1, 1 - q)
                if runs(k, q, 0):
                    sp.wait_ge(x1_ready, it + 1)
                    sp.dma_start(x1_dram[:, bass.ds(it * GB, GB), :], x1[q]).then_inc(x1_spilled[q], 16)
                if runs(k, q, 3):
                    sp.wait_ge(out_ready, it - 3 + 1)
                    sp.dma_start(out_rows[:, bass.ds((it - 3) * GB, GB), :], out_sb).then_inc(out_written, 16)

            third_phase(sp, body, peel_end=1)
            sp.wait_ge(out_written, 16 * GROUPS)

        @block.gpsimd
        def _(pool):
            nc.gpsimd.memset(vec_rows, 0.0).then_inc(consts_done, 1)
            nc.gpsimd.memset(ident[:], 0.0).then_inc(consts_done, 1)
            nc.gpsimd.memset(ident16[:], 0.0).then_inc(consts_done, 1)
            nc.gpsimd.memset(ones[:], 1.0).then_inc(consts_done, 1)
            nc.gpsimd.memset(minus_half[:], -0.5).then_inc(consts_done, 1)
            nc.gpsimd.memset(small[:], 0.0).then_inc(consts_done, 1)
            pool.wait_ge(consts_done, 6)
            for m in (ident, ident16):
                nc.gpsimd.affine_select(out=m[:], in_=m[:], compare_op=ALU.not_equal, fill=1.0, base=0,
                                        pattern=[[-1, P]], channel_multiplier=1).then_inc(consts_done, 1)
            pool.wait_ge(prep_dve, DEG_STEP)
            nc.gpsimd.tensor_tensor(small[:, 4:5], small[:, 3:4], minus_half[:, 0:1], ALU.pow)\
                .then_inc(dinv_done, 1)
            for n, cols in enumerate((slice(0, H1), slice(H1, H1 + 1))):
                pool.wait_ge(bn_moments, H1 if n == 0 else H1 + 1)
                width = cols.stop - cols.start
                nc.gpsimd.tensor_scalar(bn_rstd[:, cols], mean_var[:, cols, 1], EPS, 1.0, ALU.add, ALU.mult)\
                    .then_inc(bn_rstd_done, 1)
                pool.wait_ge(bn_rstd_done, 2 * n + 1)
                nc.gpsimd.tensor_tensor(bn_rstd[:, cols], bn_rstd[:, cols], minus_half[:, 0:width], ALU.pow)\
                    .then_inc(bn_rstd_done, 1)

            def normalise(g, which, lns_before, src, dst, moments, ready):
                mv, coef = ln_mv[:, which], ln_coef[:, which]
                pool.wait_ge(moments, MOMENT_STEPS * (g + 1))
                nc.gpsimd.tensor_tensor(coef[:, 2, :], mv[:, 0, :], minus_half[:], ALU.mult).then_inc(ln_step, 1)
                nc.gpsimd.tensor_scalar(coef[:, 0, :], mv[:, 1, :], 1.0 / P, EPS, ALU.mult, ALU.add)\
                    .then_inc(ln_step, 1)
                pool.wait_ge(ln_step, 3 * lns_before + 2)
                nc.gpsimd.tensor_tensor(coef[:, 1, :], coef[:, 0, :], minus_half[:], ALU.pow).then_inc(ln_step, 1)
                pool.wait_ge(ln_step, 3 * lns_before + 3)
                pool.sem_inc(coef_seen, 1)
                for b in range(GB):
                    last = nc.gpsimd.tensor_scalar(dst[:, b, :], src[:, b, :], coef[:, 2, b:b + 1],
                                                   coef[:, 1, b:b + 1], ALU.add, ALU.mult)
                last.then_inc(ready, 1)

            def body(k, q):
                it = 2 * k + q
                before_1 = min(it, GROUPS) if isinstance(k, int) else it
                before_2 = max(it - 3, 0) if isinstance(k, int) else it - 3
                if runs(k, q, 3):
                    wait(pool, out_written, 16 * (it - 3))
                    normalise(it - 3, 1, before_1 + before_2, y2, out_sb, y2_moments, out_ready)
                    before_2 = before_2 + 1
                if runs(k, q, 0):
                    wait(pool, x1_spilled[q], 16 * k)
                    wait(pool, u0_summed, 2 * (it - 1))
                    normalise(it, 0, before_1 + before_2, y, x1[q], y_moments, x1_ready)

            third_phase(pool, body)

        @block.tensor
        def _(pe):
            pe.wait_ge(consts_done, N_CONSTS)
            pe.wait_ge(ld_adj, 16)
            nc.tensor.transpose(ps[:, 0, 0:P], adj_n[:], ident[:]).then_inc(prep_pe, 1)
            pe.wait_ge(ld_w12, 32)
            for j in range(4):
                last = nc.tensor.transpose(ps[:, 3, j * P:(j + 1) * P], w12_rows[:, j, :], ident[:])
            last.then_inc(prep_pe, 1)
            pe.wait_ge(prep_dve, ADJT_STEP)
            nc.tensor.matmul(ps[:, 2, 0:P], ones[:], adjT[:], start=True, stop=True).then_inc(prep_pe, 1)
            pe.wait_ge(ld_vec, 8 * 16)
            nc.tensor.transpose(ps[:, 1, 0:P], vec_rows, ident[:]).then_inc(prep_pe, 1)
            pe.wait_ge(prep_dve, SCALED_STEP)
            nc.tensor.transpose(ps[:, 4, 0:P], tmp_pp[:], ident[:]).then_inc(prep_pe, 1)
            pe.wait_ge(prep_dve, PREP_STEPS)

            def aggregate(k, j):
                c, q = 4 * k + j, j % 4
                pe.wait_ge(x_loaded[q], 16 * (k + j // 4 + 1))
                wait(pe, agg_copied, c - 1)
                for b in range(CB):
                    last = nc.tensor.matmul(ps[:, q % 2, b * P:(b + 1) * P], x_in[:, q, b * P:(b + 1) * P],
                                            ahatT[:], start=True, stop=True)
                last.then_inc(agg_summed, 1)

            def channels(c, q):
                pe.wait_ge(agg_copied, c + 1)
                wait(pe, chan_stored, H1 * (c - 1))
                for h in range(H1):
                    nc.tensor.matmul(ps[:, 2 + 2 * (q % 2) + h, :], w1T[:, h, :], aggT[:, q % 2, :],
                                     start=True, stop=True).then_inc(chan_summed, 1)

            aggregate(0, 0)
            for q in range(4):
                aggregate(0, q + 1)
                channels(q, q)
            with pe.Fori(1, CHUNKS // 4 - 1) as k:
                for q in range(4):
                    aggregate(k, q + 1)
                    channels(k * 4 + q, q)
            for c in range(CHUNKS - 4, CHUNKS):
                if c + 1 < CHUNKS:
                    aggregate(c // 4, c % 4 + 1)
                channels(c, c % 4)

            pe.wait_ge(ld_lstm, 32)
            for job in range(W_JOBS):
                wait(pe, w_lo_done, job - 1)
                for j in range(4):
                    last = nc.tensor.transpose(ps[:, 6 + job % 2, j * P:(j + 1) * P],
                                               lstm_rows[:, job * 4 + j, :], ident[:])
                last.then_inc(w_turned, 1)

            def second_layer(c, q):
                pe.wait_ge(relu_done, H1 * (c + 1))
                wait(pe, out_stored, c - 1)
                for h in range(H1):
                    last = nc.tensor.matmul(ps[:, q % 2, :], w2T[:, h, :], relu1[:, q % 2, h, :],
                                            start=(h == 0), stop=(h == H1 - 1))
                last.then_inc(out_summed, 1)

            chunks_by_four(pe, second_layer)

            def lstm_step(th, g, s, rows16):
                step = th.steps[s]
                n = step["nb"] * step["rows"]
                job0 = sum(len(gates_of(t)) for t in th.steps[:s])
                x_hi, x_lo = rows_of(rows16[:, 0], step), rows_of(rows16[:, 1], step)
                h_hi, h_lo = flat(th.hid16[:, 0], step), flat(th.hid16[:, 1], step)
                for j, gate in enumerate(gates_of(step)):
                    job = job0 + j
                    wait(pe, th.gate_done, g * th.n_gates + max(job - GATE_BANKS + 1, 0))
                    acc = flat(ps[:, th.bank + job % GATE_BANKS, :], step)
                    col = (4 * (step["p"] - 1) + gate) * P
                    w_hi, w_lo = wih[:, 0, col:col + P], wih[:, 1, col:col + P]
                    passes = [(w_hi, x_hi), (w_hi, x_lo), (w_lo, x_hi)]
                    if not step["first"]:
                        col -= 4 * P
                        w_hi, w_lo = whh[:, 0, col:col + P], whh[:, 1, col:col + P]
                        passes += [(w_hi, h_hi), (w_hi, h_lo), (w_lo, h_hi)]
                    for m, (w, v) in enumerate(passes):
                        last = nc.tensor.matmul(acc, w, v, start=(m == 0), stop=(m == len(passes) - 1))
                    last.then_inc(th.gate_summed, 1)

            def turn_z(g):
                pe.wait_ge(z_ready, g + 1)
                for b in range(GB):
                    if b == 0:
                        wait(pe, gnn_lo_done, 2 * g)
                        wait(pe, y2_ready, 2 * finished(g))
                    last = nc.tensor.transpose(ps[:, TURN + b // CB, b % CB * P:(b % CB + 1) * P],
                                               zT[:, b, :], ident[:])
                    if b % CB == CB - 1:
                        last.then_inc(z_turned, 1)

            def finished(g):
                return max(g - 2, 0) if isinstance(g, int) else g - 2

            def turn_h(g, par):
                pe.wait_ge(late.lo_done, late.steps_before(g + 1, 0))
                wait(pe, gnn_lo_done, 2 * (g + 3) if not isinstance(g, int) else 2 * min(g + 3, GROUPS))
                for b in range(GB):
                    acc = ps[:, TURN + b // CB, b % CB * P:(b % CB + 1) * P]
                    nc.tensor.matmul(acc, h16[par][:, 0, b, :], ident16[:], start=True, stop=False)
                    last = nc.tensor.matmul(acc, h16[par][:, 1, b, :], ident16[:], start=False, stop=True)
                    if b % CB == CB - 1:
                        last.then_inc(h_turned, 1)

            def half(h):
                return ps[:, TURN + h, :]

            def mix_u0(g, par):
                pe.wait_ge(x1_ready, g + 1)
                for b in range(GB):
                    if b % CB == 0:
                        pe.wait_ge(y_ready, 2 * g + b // CB + 1)
                    last = nc.tensor.matmul(half(b // CB)[:, b % CB * P:(b % CB + 1) * P], x1[par][:, b, :],
                                            adjT[:], start=True, stop=True)
                    if b % CB == CB - 1:
                        last.then_inc(u0_summed, 1)

            def layer_h0(g):
                for h in range(2):
                    pe.wait_ge(u0_copied, 2 * g + h + 1)
                    nc.tensor.matmul(half(h), bias_l[:, 0, :], bias_r[:].rearrange("p b n -> p (b n)"),
                                     start=True, stop=False)
                    nc.tensor.matmul(half(h), wg0_sb[:], u0T[:, h * CB:(h + 1) * CB, :].rearrange(
                        "p b n -> p (b n)"), start=False, stop=True).then_inc(h0_summed, 1)

            def layer_u1(g):
                for b in range(GB):
                    if b % CB == 0:
                        pe.wait_ge(h0_copied, 2 * g + b // CB + 1)
                    last = nc.tensor.matmul(half(b // CB)[:, b % CB * P:(b % CB + 1) * P], h0T[:, b, :],
                                            wg1_sb[:], start=True, stop=True)
                    if b % CB == CB - 1:
                        last.then_inc(u1_summed, 1)

            def mix_gnn(g):
                for h in range(2):
                    pe.wait_ge(u1_copied, 2 * g + h + 1)
                    nc.tensor.matmul(half(h), bias_l[:, 1, :], bias_r[:].rearrange("p b n -> p (b n)"),
                                     start=True, stop=False)
                    for b in range(CB):
                        last = nc.tensor.matmul(half(h)[:, b * P:(b + 1) * P], u1[:, h * CB + b, :], adjT[:],
                                                start=False, stop=(b == CB - 1))
                    last.then_inc(gnn_summed, 1)

            def body(k, q):
                it = 2 * k + q

                def late_step(s):
                    if runs(k, q, 2):
                        g = it - 2
                        if s == 0:
                            pe.wait_ge(early.lo_done, early.steps_before(g + 1, 0))
                        else:
                            pe.wait_ge(late.lo_done, late.steps_before(g, s))
                        lstm_step(late, g, s, h16[q])

                def early_step(s):
                    if runs(k, q, 1):
                        g = it - 1
                        if s < 2:
                            pe.wait_ge(gnn_lo_done, 2 * g + s + 1)
                            lstm_step(early, g, s, gnn16)
                        else:
                            pe.wait_ge(early.lo_done, early.steps_before(g, s))
                            lstm_step(early, g, s, h16[1 - q])

                if runs(k, q, 3):
                    turn_h(it - 3, 1 - q)
                late_step(0)
                early_step(0)
                if runs(k, q, 0):
                    turn_z(it)
                late_step(1)
                early_step(1)
                late_step(2)
                early_step(2)
                late_step(3)
                if runs(k, q, 0):
                    mix_u0(it, q)
                early_step(3)
                late_step(4)
                if runs(k, q, 0):
                    layer_h0(it)
                late_step(5)
                if runs(k, q, 0):
                    layer_u1(it)
                late_step(6)
                if runs(k, q, 0):
                    mix_gnn(it)

            third_phase(pe, body)

        @block.scalar
        def _(act):
            act.wait_ge(prep_dve, PREP_STEPS)

            def copy_agg(c, q):
                act.wait_ge(agg_summed, c + 1)
                wait(act, chan_summed, H1 * (c - 1))
                nc.scalar.activation(aggT[:, q % 2, :], ps[:, q % 2, :], ACT.Copy).then_inc(agg_copied, 1)

            def store_channels(c, q):
                for h in range(H1):
                    act.wait_ge(chan_summed, H1 * c + h + 1)
                    nc.scalar.activation(store[:, h, bass.ds(c * BANK, BANK)], ps[:, 2 + 2 * (q % 2) + h, :],
                                         ACT.Identity, bias=vec[:, VB1 + h:VB1 + h + 1])\
                        .then_inc(chan_stored, 1)

            copy_agg(0, 0)
            for q in range(4):
                copy_agg(q + 1, (q + 1) % 4)
                store_channels(q, q)
            with act.Fori(1, CHUNKS // 4 - 1) as k:
                for q in range(4):
                    copy_agg(k * 4 + q + 1, (q + 1) % 4)
                    store_channels(k * 4 + q, q)
            for c in range(CHUNKS - 4, CHUNKS):
                if c + 1 < CHUNKS:
                    copy_agg(c + 1, (c + 1) % 4)
                store_channels(c, c % 4)

            for job in range(W_JOBS):
                act.wait_ge(w_turned, job + 1)
                nc.scalar.activation(split_weights(job)[:, 0, :], ps[:, 6 + job % 2, :], ACT.Copy,
                                     scale=W_SCALE).then_inc(w_hi_done, 1)

            act.wait_ge(bn_ready, 1)

            def relu_chunk(c, q):
                wait(act, out_summed, c - 1)
                for h in range(H1):
                    nc.scalar.activation(relu1[:, q % 2, h, :], store[:, h, bass.ds(c * BANK, BANK)], ACT.Relu,
                                         bias=bn_shift[:, h:h + 1], scale=bn_scale[:, h:h + 1])\
                        .then_inc(relu_done, 1)

            chunks_by_four(act, relu_chunk)

            act.wait_ge(bn_ready, 2)

            def gates(th, g, s):
                step = th.steps[s]
                n = step["nb"] * step["rows"]
                job0 = sum(len(gates_of(t)) for t in th.steps[:s])
                for j, gate in enumerate(gates_of(step)):
                    job = job0 + j
                    act.wait_ge(th.gate_summed, g * th.n_gates + job + 1)
                    used = th.hid_done if gate == O else th.cell_done
                    wait(act, used, th.steps_before(g, s))
                    row = 4 * (step["p"] - 1) + gate
                    nc.scalar.activation(th.acts[:, gate, 0:n], ps[:, th.bank + job % GATE_BANKS, 0:n],
                                         ACT.Tanh if gate == G else ACT.Sigmoid,
                                         bias=gate_bias[:, row:row + 1], scale=1.0 / W_SCALE)\
                        .then_inc(th.gate_done, 1)

            def tanh_cell(th, g, s):
                n = th.steps[s]["nb"] * th.steps[s]["rows"]
                act.wait_ge(th.cell_done, th.steps_before(g, s) + 1)
                nc.scalar.activation(th.tanh_c[:, 0:n], th.cell[:, 0:n], ACT.Tanh).then_inc(th.tanh_done, 1)

            def evacuate(g, summed, dst, func, done, used=None, per_group=2):
                for h in range(2):
                    act.wait_ge(summed, 2 * g + h + 1)
                    if used is not None:
                        wait(act, used, per_group * g)
                    nc.scalar.activation(dst[:, h * CB:(h + 1) * CB, :].rearrange("p b n -> p (b n)"),
                                         ps[:, TURN + h, :], func).then_inc(done, 1)

            def body(k, q):
                it = 2 * k + q

                def late_part(fn, s):
                    if runs(k, q, 2):
                        fn(late, it - 2, s)

                def early_part(fn, s):
                    if runs(k, q, 1):
                        fn(early, it - 1, s)

                if runs(k, q, 0):
                    wait(act, z_turned, 2 * it)
                    nc.scalar.activation(zT.rearrange("p b n -> p (b n)"), store[:, 0, bass.ds(it * GCOLS, GCOLS)],
                                         ACT.Identity, bias=bn_shift[:, H1:H1 + 1],
                                         scale=bn_scale[:, H1:H1 + 1]).then_inc(z_ready, 1)
                for s in range(3):
                    late_part(gates, s)
                    early_part(gates, s)
                    late_part(tanh_cell, s)
                    early_part(tanh_cell, s)
                late_part(gates, 3)
                if runs(k, q, 0):
                    evacuate(it, u0_summed, u0T, ACT.Copy, u0_copied, h0_summed)
                late_part(tanh_cell, 3)
                early_part(gates, 3)
                late_part(gates, 4)
                early_part(tanh_cell, 3)
                if runs(k, q, 0):
                    evacuate(it, h0_summed, h0T, ACT.Relu, h0_copied, u1_summed)
                late_part(tanh_cell, 4)
                late_part(gates, 5)
                if runs(k, q, 0):
                    evacuate(it, u1_summed, u1, ACT.Copy, u1_copied, gnn_summed)
                late_part(tanh_cell, 5)
                late_part(gates, 6)
                if runs(k, q, 0):
                    evacuate(it, gnn_summed, gnn16[:, 0], ACT.Relu, gnn_hi_done, early.gate_summed,
                             early.n_gates)
                late_part(tanh_cell, 6)

            third_phase(act, body)

        @block.vector
        def _(dve):
            steps = [0]

            def link(instruction):
                instruction.then_inc(prep_dve, 1)
                steps[0] += 1
                dve.wait_ge(prep_dve, steps[0])

            ident_col = ident[:, 0:1]
            rsum, csum, diag, deg, dinv, sel02, sel01 = (small[:, k:k + 1] for k in range(7))
            dve.wait_ge(consts_done, N_CONSTS)
            dve.wait_ge(prep_pe, 1)
            link(nc.vector.tensor_copy(adjT[:], ps[:, 0, 0:P]))
            assert steps[0] == ADJT_STEP
            link(nc.vector.tensor_tensor(a_norm[:], adj_n[:], ident[:], ALU.add))
            link(nc.vector.tensor_tensor(tmp_pp[:], adjT[:], ident[:], ALU.add))
            link(nc.vector.reduce_sum(rsum, a_norm[:], AX_X))
            link(nc.vector.reduce_sum(csum, tmp_pp[:], AX_X))
            link(nc.vector.tensor_tensor(tmp_pp[:], a_norm[:], ident[:], ALU.mult))
            link(nc.vector.reduce_sum(diag, tmp_pp[:], AX_X))
            link(nc.vector.tensor_tensor(deg, rsum, csum, ALU.add))
            link(nc.vector.tensor_tensor(deg, deg, diag, ALU.subtract))
            assert steps[0] == DEG_STEP
            dve.wait_ge(dinv_done, 1)
            link(nc.vector.tensor_scalar(tmp_pp[:], a_norm[:], dinv, None, ALU.mult))
            assert steps[0] == SCALED_STEP
            dve.wait_ge(prep_pe, 2)
            for h in range(H1):
                link(nc.vector.tensor_copy(w1T[:, h, :], ps[:, 3, h * P:(h + 1) * P]))
                link(nc.vector.tensor_copy(w2T[:, h, :], ps[:, 3, (2 + h) * P:(3 + h) * P]))
            dve.wait_ge(prep_pe, 3)
            link(nc.vector.tensor_tensor(sel02, ident[:, 0:1], ident[:, 2:3], ALU.add))
            link(nc.vector.tensor_tensor(sel01, ident[:, 0:1], ident[:, 1:2], ALU.add))
            link(nc.vector.tensor_copy(split16[:, 0, :], ps[:, 2, 0:P]))
            link(nc.vector.tensor_tensor(split16[:, 1, :], ps[:, 2, 0:P], split16[:, 0, :], ALU.subtract))
            link(nc.vector.tensor_scalar(split16[:, 1, :], split16[:, 1, :], ident[:, 1:2], None, ALU.mult))
            for b in range(CB):
                link(nc.vector.scalar_tensor_tensor(bias_r[:, b, :], split16[:, 0, :], sel02, split16[:, 1, :],
                                                    ALU.mult, ALU.add))
            dve.wait_ge(ld_bg, 32)
            for n in range(2):
                link(nc.vector.tensor_copy(split16[:, 0, :], bg_rows[:, n, :]))
                link(nc.vector.tensor_tensor(split16[:, 1, :], bg_rows[:, n, :], split16[:, 0, :], ALU.subtract))
                link(nc.vector.tensor_scalar(split16[:, 1, :], split16[:, 1, :], ident[:, 2:3], None, ALU.mult))
                link(nc.vector.scalar_tensor_tensor(bias_l[:, n, :], split16[:, 0, :], sel01, split16[:, 1, :],
                                                    ALU.mult, ALU.add))
            dve.wait_ge(prep_pe, 4)
            link(nc.vector.tensor_copy(vec[:], ps[:, 1, 0:P]))
            link(nc.vector.tensor_tensor(gate_bias[:], vec[:, VIH:VIH + NG], vec[:, VHH:VHH + NG], ALU.add))
            dve.wait_ge(prep_pe, 5)
            link(nc.vector.tensor_scalar(ahatT[:], ps[:, 4, 0:P], dinv, None, ALU.mult))
            assert steps[0] == PREP_STEPS

            def channel_stats(c, q):
                for h in range(H1):
                    dve.wait_ge(chan_stored, H1 * c + h + 1)
                    nc.vector.bn_stats(st1[:, h, bass.ds(c, 1), :].rearrange("p c s -> p (c s)"),
                                       store[:, h, bass.ds(c * BANK, BANK)]).then_inc(chan_stats, 1)

            chunks_by_four(dve, channel_stats)

            def batch_norm(first, n, rstd_count, gamma, beta, step0):
                cols = slice(first, first + n)
                dve.wait_ge(bn_rstd_done, rstd_count)
                dve.wait_ge(bn_moments, first + n)
                nc.vector.tensor_tensor(bn_scale[:, cols], vec[:, gamma:gamma + n], bn_rstd[:, cols], ALU.mult)\
                    .then_inc(bn_step, 1)
                dve.wait_ge(bn_step, step0 + 1)
                nc.vector.tensor_tensor(bn_shift[:, cols], mean_var[:, cols, 0], bn_scale[:, cols], ALU.mult)\
                    .then_inc(bn_step, 1)
                dve.wait_ge(bn_step, step0 + 2)
                nc.vector.tensor_tensor(bn_shift[:, cols], vec[:, beta:beta + n], bn_shift[:, cols],
                                        ALU.subtract).then_inc(bn_ready, 1)

            dve.wait_ge(chan_stats, H1 * CHUNKS)
            for h in range(H1):
                nc.vector.bn_aggr(mean_var[:, h, :], st1[:, h, :, :].rearrange("p c s -> p (c s)"))\
                    .then_inc(bn_moments, 1)
            batch_norm(0, H1, 2, VG1, VBE1, 0)

            for job in range(W_JOBS):
                dve.wait_ge(w_hi_done, job + 1)
                parts = split_weights(job)
                nc.vector.scalar_tensor_tensor(parts[:, 1, :], ps[:, 6 + job % 2, :], W_SCALE, parts[:, 0, :],
                                               ALU.mult, ALU.subtract).then_inc(w_lo_done, 1)

            def store_out(c, q):
                dve.wait_ge(out_summed, c + 1)
                nc.vector.tensor_scalar(store[:, 0, bass.ds(c * BANK, BANK)], ps[:, q % 2, :],
                                        vec[:, VB2:VB2 + 1], None, ALU.add).then_inc(out_stored, 1)
                dve.wait_ge(out_stored, c + 1)
                nc.vector.bn_stats(st2[:, bass.ds(c, 1), :].rearrange("p c s -> p (c s)"),
                                   store[:, 0, bass.ds(c * BANK, BANK)]).then_inc(out_stats, 1)

            chunks_by_four(dve, store_out)
            dve.wait_ge(out_stats, CHUNKS)
            nc.vector.bn_aggr(mean_var[:, H1, :], st2[:].rearrange("p c s -> p (c s)")).then_inc(bn_moments, 1)
            batch_norm(H1, 1, 4, VG2, VBE2, 2)

            def cell(th, g, s):
                step = th.steps[s]
                n = step["nb"] * step["rows"]
                gate0 = th.gates_before(g, s)
                i, f, gg = (th.acts[:, gate, 0:n] for gate in (I, F, G))
                dve.wait_ge(th.gate_done, gate0 + 2)
                if step["first"]:
                    wait(dve, th.tanh_done, th.steps_before(g, s))
                    nc.vector.tensor_tensor(th.cell[:, 0:n], i, gg, ALU.mult).then_inc(th.cell_done, 1)
                    return
                nc.vector.tensor_tensor(th.ig[:, 0:n], i, gg, ALU.mult).then_inc(th.parts, 1)
                dve.wait_ge(th.gate_done, gate0 + 3)
                nc.vector.tensor_tensor(th.fc[:, 0:n], f, th.cell[:, 0:n], ALU.mult).then_inc(th.parts, 1)
                dve.wait_ge(th.parts, th.parts_before(g, s) + 2)
                nc.vector.tensor_tensor(th.cell[:, 0:n], th.ig[:, 0:n], th.fc[:, 0:n], ALU.add)\
                    .then_inc(th.cell_done, 1)

            def hidden(th, g, s, rows16):
                step = th.steps[s]
                n = step["nb"] * step["rows"]
                done = th.steps_before(g, s) + 1
                dve.wait_ge(th.gate_done, th.gates_before(g, s) + len(gates_of(step)))
                dve.wait_ge(th.tanh_done, done)
                wait(dve, th.lo_done, done - 1)
                nc.vector.tensor_tensor(th.hid[:, 0:n], th.acts[:, O, 0:n], th.tanh_c[:, 0:n], ALU.mult)\
                    .then_inc(th.hid_done, 1)
                hid = flat(th.hid, step)
                if step["last"]:
                    hi, lo = rows_of(rows16[:, 0], step), rows_of(rows16[:, 1], step)
                else:
                    hi, lo = flat(th.hid16[:, 0], step), flat(th.hid16[:, 1], step)
                dve.wait_ge(th.hid_done, done)
                nc.vector.tensor_copy(hi, hid).then_inc(th.hi_done, 1)
                dve.wait_ge(th.hi_done, done)
                nc.vector.tensor_tensor(lo, hid, hi, ALU.subtract).then_inc(th.lo_done, 1)

            def residual(g, turned, other, dst, ready, stats, moments, which):
                for h in range(2):
                    dve.wait_ge(turned, 2 * g + h + 1)
                    nc.vector.tensor_tensor(
                        dst[:, h * CB:(h + 1) * CB, :].rearrange("p b n -> p (b n)"), ps[:, TURN + h, :],
                        other[:, h * CB:(h + 1) * CB, :].rearrange("p b n -> p (b n)"), ALU.add)\
                        .then_inc(ready, 1)
                for b in range(GB):
                    if b % CB == 0:
                        dve.wait_ge(ready, 2 * g + b // CB + 1)
                    nc.vector.bn_stats(ln_stats[:, which, b, :], dst[:, b, :]).then_inc(stats, 1)
                (even, even_m2), (odd, odd_m2) = (
                    (ln_stats[:, which, :, k], ln_stats[:, which, :, k + 1]) for k in (1, 4))
                mean2, var, diff = (ln_mv[:, which, k, :] for k in range(3))
                dve.wait_ge(stats, GB * (g + 1))
                before = MOMENT_STEPS * g
                nc.vector.tensor_tensor(diff, even, odd, ALU.subtract).then_inc(moments, 1)
                nc.vector.tensor_tensor(mean2, even, odd, ALU.add).then_inc(moments, 1)
                nc.vector.tensor_tensor(var, even_m2, odd_m2, ALU.add).then_inc(moments, 1)
                dve.wait_ge(moments, before + 1)
                nc.vector.scalar_tensor_tensor(diff, diff, P / 4.0, diff, ALU.mult, ALU.mult)\
                    .then_inc(moments, 1)
                dve.wait_ge(moments, before + 4)
                nc.vector.tensor_tensor(var, var, diff, ALU.add).then_inc(moments, 1)

            def body(k, q):
                it = 2 * k + q

                def late_part(fn, s, *rows):
                    if runs(k, q, 2):
                        fn(late, it - 2, s, *rows)

                def early_part(fn, s, *rows):
                    if runs(k, q, 1):
                        fn(early, it - 1, s, *rows)

                rows_late, rows_early = h16[q], h16[1 - q]
                for s in range(3):
                    late_part(cell, s)
                    if s == 0 and runs(k, q, 3):
                        g = it - 3
                        wait(dve, out_ready, g)
                        dve.wait_ge(x1_reloaded, 16 * (g + 1))
                        residual(g, h_turned, x1_back, y2, y2_ready, y2_stats, y2_moments, 1)
                    early_part(cell, s)
                    late_part(hidden, s, rows_late)
                    if s == 0 and runs(k, q, 3):
                        dve.wait_ge(h_turned, 2 * (it - 2))
                    early_part(hidden, s, rows_early)
                    if s == 0 and runs(k, q, 0):
                        wait(dve, x1_ready, it)
                        dve.wait_ge(res_loaded[q], 16 * (k + 1))
                        residual(it, z_turned, x_res[q], y, y_ready, y_stats, y_moments, 0)
                late_part(cell, 3)
                late_part(hidden, 3, rows_late)
                early_part(cell, 3)
                late_part(cell, 4)
                early_part(hidden, 3, rows_early)
                late_part(hidden, 4, rows_late)
                late_part(cell, 5)
                late_part(hidden, 5, rows_late)
                late_part(cell, 6)
                if runs(k, q, 0):
                    for h in range(2):
                        dve.wait_ge(gnn_hi_done, 2 * it + h + 1)
                        rows = slice(h * CB, (h + 1) * CB)
                        nc.vector.scalar_tensor_tensor(
                            gnn16[:, 1, rows, :].rearrange("p b n -> p (b n)"), ps[:, TURN + h, :], 0.0,
                            gnn16[:, 0, rows, :].rearrange("p b n -> p (b n)"), ALU.max, ALU.subtract)\
                            .then_inc(gnn_lo_done, 1)
                late_part(hidden, 6, rows_late)

            third_phase(dve, body)


ADJT_STEP = 1
DEG_STEP = 9
SCALED_STEP = 10
PREP_STEPS = 34

_INS = ['x', 'adj', 'L0_gnn_W1', 'L0_gnn_b1', 'L0_gnn_g1', 'L0_gnn_be1', 'L0_gnn_W2', 'L0_gnn_b2',
        'L0_gnn_g2', 'L0_gnn_be2', 'L1_gnn_Wg0', 'L1_gnn_bg0', 'L1_gnn_Wg1', 'L1_gnn_bg1',
        'L1_gnn_Wih', 'L1_gnn_Whh', 'L1_gnn_bih', 'L1_gnn_bhh']
_OUTS = [((128, 128, 128), 'float32')]


def kernel(**inputs):
    import numpy as _np
    import concourse.bacc as _bacc
    from concourse import mybir as _mybir
    from concourse.bass_utils import run_bass_kernel_spmd as _run

    nc = _bacc.Bacc("TRN2", target_bir_lowering=False, num_devices=1)
    arrays, args = {}, []
    for name in _INS:
        a = _np.ascontiguousarray(inputs[name])
        arrays[f"in_{name}_dram"] = a
        args.append(nc.dram_tensor(f"in_{name}_dram", a.shape, _mybir.dt.from_np(a.dtype), kind="ExternalInput").ap())
    for i, (shape, dtype) in enumerate(_OUTS):
        dt = _mybir.dt.from_np(_np.dtype(dtype))
        args.append(nc.dram_tensor(f"out_{i}_dram", shape, dt, kind="ExternalOutput").ap())
    resnorm_gnn_kernel(nc, *args)
    r = _run(nc, [arrays], core_ids=[0])
    got = tuple(r.results[0][f"out_{i}_dram"] for i in range(len(_OUTS)))
    return got[0]
```
